# Optimizing a Trainium2 kernel written in Bass

```python
import numpy as np
import jax
import jax.numpy as jnp

def _softmax(x, axis=-1):
    return jax.nn.softmax(x, axis=axis)

def _gelu(x):
    return jax.nn.gelu(x, approximate=True)

def _silu(x):
    return jax.nn.silu(x)

def _sigmoid(x):
    return jax.nn.sigmoid(x)

def _layernorm(x, axis=-1, eps=1e-05):
    m = jnp.mean(x, axis=axis, keepdims=True)
    v = jnp.var(x, axis=axis, keepdims=True)
    return (x - m) / jnp.sqrt(v + eps)

def _scatter_add(tgt, idx, src, axis=0):
    return tgt.at[idx].add(src)

def _segment_sum(src, seg, n):
    return jax.ops.segment_sum(src, seg, n)
kernel_name = 'mk_adaln_d1_jaxref_r8_dc744c'

def setup_inputs(seed: int=0):
    np.random.seed(seed)
    _w = jnp.asarray

    def _L0_attn_setup():
        import jax, jax.numpy as jnp
        import numpy as np
        DIM = 128
        N_HEADS = 16
        HEAD_DIM = DIM // N_HEADS
        D_LATENT = 32
        B, T = (1, 512)
        key = jax.random.key(seed)
        ks = jax.random.split(key, 6)
        s = 0.02
        return {'x': jax.random.normal(ks[0], (B, T, DIM), dtype=jnp.float32), 'W_DKV': jax.random.normal(ks[1], (DIM, D_LATENT), dtype=jnp.float32) * s, 'W_UK': jax.random.normal(ks[2], (D_LATENT, DIM), dtype=jnp.float32) * s, 'W_UV': jax.random.normal(ks[3], (D_LATENT, DIM), dtype=jnp.float32) * s, 'W_UQ': jax.random.normal(ks[4], (DIM, DIM), dtype=jnp.float32) * s, 'W_O': jax.random.normal(ks[5], (DIM, DIM), dtype=jnp.float32) * s}
    _L0_attn_in = _L0_attn_setup()

    def _L0_ffn_setup():
        import jax, jax.numpy as jnp
        import numpy as np
        DIM = 128
        DEPTH = 2
        HEADS = 8
        DIM_HEAD = 64
        WINDOW = 64
        INNER = HEADS * DIM_HEAD
        HID = int(DIM * 4 * 2 / 3)
        B, N = (2, 1024)
        QK_SCALE = 8.0

        def shift_token(t):
            t1, t2 = jnp.split(t, 2, axis=-1)
            t2 = jnp.pad(t2, ((0, 0), (1, 0), (0, 0)))[:, :-1]
            return jnp.concatenate([t1, t2], axis=-1)

        def l2norm(t):
            return t / jnp.clip(jnp.linalg.norm(t, axis=-1, keepdims=True), 1e-12)

        def rotate_half(x):
            x1, x2 = jnp.split(x, 2, axis=-1)
            return jnp.concatenate([-x2, x1], axis=-1)

        def rotary_xpos(q, k):
            n = q.shape[-2]
            half_idx = jnp.arange(0, DIM_HEAD, 2, dtype=jnp.float32)
            inv_freq = 1.0 / 10000.0 ** (half_idx / DIM_HEAD)
            t = jnp.arange(n, dtype=jnp.float32)
            freqs = t[:, None] * inv_freq[None, :]
            freqs = jnp.concatenate([freqs, freqs], axis=-1)
            base = (half_idx + 0.4 * DIM_HEAD) / (1.4 * DIM_HEAD)
            power = (t - n // 2) / float(WINDOW // 2)
            scale = base[None, :] ** power[:, None]
            scale = jnp.concatenate([scale, scale], axis=-1)
            cos, sin = (jnp.cos(freqs), jnp.sin(freqs))
            q = q * cos * scale + rotate_half(q) * sin * scale
            k = k * cos / scale + rotate_half(k) * sin / scale
            return (q, k)

        def local_attention(q, k, v):
            b, h, n, d = q.shape
            w = n // WINDOW
            bq = q.reshape(b, h, w, WINDOW, d) * QK_SCALE
            bk = k.reshape(b, h, w, WINDOW, d)
            bv = v.reshape(b, h, w, WINDOW, d)

            def look_around(t):
                p = jnp.pad(t, ((0, 0), (0, 0), (1, 0), (0, 0), (0, 0)))
                return jnp.concatenate([p[:, :, :w], p[:, :, 1:]], axis=3)
            bk, bv = (look_around(bk), look_around(bv))
            bt = jnp.arange(n).reshape(w, WINDOW)
            btp = jnp.pad(bt, ((1, 0), (0, 0)), constant_values=-1)
            btk = jnp.concatenate([btp[:w], btp[1:]], axis=1)
            sim = jnp.einsum('bhwid,bhwjd->bhwij', bq, bk)
            i = bt[:, :, None]
            j = btk[:, None, :]
            mask = (i < j) | (i > j + WINDOW) | (j == -1)
            sim = jnp.where(mask, -jnp.finfo(sim.dtype).max, sim)
            attn = jax.nn.softmax(sim, axis=-1)
            out = jnp.einsum('bhwij,bhwjd->bhwid', attn, bv)
            return out.reshape(b, h, n, d)

        def _layer(x, wqkv, qs, ksc, wo, lg, lb, w1, b1, w2, b2):
            b, n, _ = x.shape
            h = shift_token(x)
            qkv = h @ wqkv
            q, k, v = jnp.split(qkv, 3, axis=-1)
            to_heads = lambda t: t.reshape(b, n, HEADS, DIM_HEAD).transpose(0, 2, 1, 3)
            q, k, v = (to_heads(q), to_heads(k), to_heads(v))
            q = l2norm(q) * qs
            k = l2norm(k) * ksc
            q, k = rotary_xpos(q, k)
            o = local_attention(q, k, v)
            o = o.transpose(0, 2, 1, 3).reshape(b, n, INNER)
            x = x + o @ wo
            h = shift_token(x)
            mu = h.mean(-1, keepdims=True)
            var = h.var(-1, keepdims=True)
            h = (h - mu) / jnp.sqrt(var + 1e-05) * lg + lb
            h = h @ w1 + b1
            a, g = jnp.split(h, 2, axis=-1)
            h = a * jax.nn.gelu(g, approximate=False)
            x = x + h @ w2 + b2
            return x
        key = jax.random.key(seed)
        ks = jax.random.split(key, 6)
        return {'x': jax.random.normal(ks[0], (B, N, DIM), jnp.float32), 'wqkv': jax.random.normal(ks[1], (DEPTH, DIM, 3 * INNER), jnp.float32) * 0.02, 'q_scale': jnp.ones((DEPTH, DIM_HEAD), jnp.float32), 'k_scale': jnp.ones((DEPTH, DIM_HEAD), jnp.float32), 'wo': jax.random.normal(ks[2], (DEPTH, INNER, DIM), jnp.float32) * 0.02, 'ln_g': jnp.ones((DEPTH, DIM), jnp.float32), 'ln_b': jnp.zeros((DEPTH, DIM), jnp.float32), 'w1': jax.random.normal(ks[3], (DEPTH, DIM, 2 * HID), jnp.float32) * 0.02, 'b1': jnp.zeros((DEPTH, 2 * HID), jnp.float32), 'w2': jax.random.normal(ks[4], (DEPTH, HID, DIM), jnp.float32) * 0.02, 'b2': jnp.zeros((DEPTH, DIM), jnp.float32)}
    _L0_ffn_in = _L0_ffn_setup()
    _L0_c = _w((lambda *s: np.random.randn(*s).astype(np.float32) * 0.05)(16, 128))
    _L0_wmod = _w((lambda *s: np.random.randn(*s).astype(np.float32) * 0.05)(128, 6 * 128) * 128 ** (-0.5))
    _d = {'L0_attn_x': _L0_attn_in['x'], 'L0_attn_W_DKV': _L0_attn_in['W_DKV'], 'L0_attn_W_UK': _L0_attn_in['W_UK'], 'L0_attn_W_UV': _L0_attn_in['W_UV'], 'L0_attn_W_UQ': _L0_attn_in['W_UQ'], 'L0_attn_W_O': _L0_attn_in['W_O'], 'L0_ffn_wqkv': _L0_ffn_in['wqkv'], 'L0_ffn_q_scale': _L0_ffn_in['q_scale'], 'L0_ffn_k_scale': _L0_ffn_in['k_scale'], 'L0_ffn_wo': _L0_ffn_in['wo'], 'L0_ffn_ln_g': _L0_ffn_in['ln_g'], 'L0_ffn_ln_b': _L0_ffn_in['ln_b'], 'L0_ffn_w1': _L0_ffn_in['w1'], 'L0_ffn_b1': _L0_ffn_in['b1'], 'L0_ffn_w2': _L0_ffn_in['w2'], 'L0_ffn_b2': _L0_ffn_in['b2'], 'L0_c': _L0_c, 'L0_wmod': _L0_wmod}
    _x0 = _d['L0_attn_x']
    _d['L0_attn_x'] = jax.random.normal(jax.random.fold_in(jax.random.key(seed), 1), (16, 512, 128), dtype=_x0.dtype)
    del _x0
    return _d

def reference(L0_attn_x, L0_attn_W_DKV, L0_attn_W_UK, L0_attn_W_UV, L0_attn_W_UQ, L0_attn_W_O, L0_ffn_wqkv, L0_ffn_q_scale, L0_ffn_k_scale, L0_ffn_wo, L0_ffn_ln_g, L0_ffn_ln_b, L0_ffn_w1, L0_ffn_b1, L0_ffn_w2, L0_ffn_b2, L0_c, L0_wmod):

    def _L0_attn_ref(x, W_DKV, W_UK, W_UV, W_UQ, W_O):
        import jax, jax.numpy as jnp
        import numpy as np
        DIM = 128
        N_HEADS = 16
        HEAD_DIM = DIM // N_HEADS
        D_LATENT = 32
        B, T = (1, 512)
        b, t, d = x.shape
        h, hd = (N_HEADS, HEAD_DIM)
        c_kv = x @ W_DKV
        k = (c_kv @ W_UK).reshape(b, t, h, hd)
        v = (c_kv @ W_UV).reshape(b, t, h, hd)
        q = (x @ W_UQ).reshape(b, t, h, hd)
        scale = 1.0 / jnp.sqrt(jnp.asarray(hd, x.dtype))
        scores = jnp.einsum('bqhd,bkhd->bhqk', q, k) * scale
        causal = jnp.tril(jnp.ones((t, t), dtype=bool))
        scores = jnp.where(causal, scores, jnp.asarray(-jnp.inf, scores.dtype))
        probs = jax.nn.softmax(scores, axis=-1)
        ctx = jnp.einsum('bhqk,bkhd->bqhd', probs, v).reshape(b, t, d)
        return ctx @ W_O

    def _L0_ffn_ref(x, wqkv, q_scale, k_scale, wo, ln_g, ln_b, w1, b1, w2, b2):
        import jax, jax.numpy as jnp
        import numpy as np
        DIM = 128
        DEPTH = 2
        HEADS = 8
        DIM_HEAD = 64
        WINDOW = 64
        INNER = HEADS * DIM_HEAD
        HID = int(DIM * 4 * 2 / 3)
        B, N = (2, 1024)
        QK_SCALE = 8.0

        def shift_token(t):
            t1, t2 = jnp.split(t, 2, axis=-1)
            t2 = jnp.pad(t2, ((0, 0), (1, 0), (0, 0)))[:, :-1]
            return jnp.concatenate([t1, t2], axis=-1)

        def l2norm(t):
            return t / jnp.clip(jnp.linalg.norm(t, axis=-1, keepdims=True), 1e-12)

        def rotate_half(x):
            x1, x2 = jnp.split(x, 2, axis=-1)
            return jnp.concatenate([-x2, x1], axis=-1)

        def rotary_xpos(q, k):
            n = q.shape[-2]
            half_idx = jnp.arange(0, DIM_HEAD, 2, dtype=jnp.float32)
            inv_freq = 1.0 / 10000.0 ** (half_idx / DIM_HEAD)
            t = jnp.arange(n, dtype=jnp.float32)
            freqs = t[:, None] * inv_freq[None, :]
            freqs = jnp.concatenate([freqs, freqs], axis=-1)
            base = (half_idx + 0.4 * DIM_HEAD) / (1.4 * DIM_HEAD)
            power = (t - n // 2) / float(WINDOW // 2)
            scale = base[None, :] ** power[:, None]
            scale = jnp.concatenate([scale, scale], axis=-1)
            cos, sin = (jnp.cos(freqs), jnp.sin(freqs))
            q = q * cos * scale + rotate_half(q) * sin * scale
            k = k * cos / scale + rotate_half(k) * sin / scale
            return (q, k)

        def local_attention(q, k, v):
            b, h, n, d = q.shape
            w = n // WINDOW
            bq = q.reshape(b, h, w, WINDOW, d) * QK_SCALE
            bk = k.reshape(b, h, w, WINDOW, d)
            bv = v.reshape(b, h, w, WINDOW, d)

            def look_around(t):
                p = jnp.pad(t, ((0, 0), (0, 0), (1, 0), (0, 0), (0, 0)))
                return jnp.concatenate([p[:, :, :w], p[:, :, 1:]], axis=3)
            bk, bv = (look_around(bk), look_around(bv))
            bt = jnp.arange(n).reshape(w, WINDOW)
            btp = jnp.pad(bt, ((1, 0), (0, 0)), constant_values=-1)
            btk = jnp.concatenate([btp[:w], btp[1:]], axis=1)
            sim = jnp.einsum('bhwid,bhwjd->bhwij', bq, bk)
            i = bt[:, :, None]
            j = btk[:, None, :]
            mask = (i < j) | (i > j + WINDOW) | (j == -1)
            sim = jnp.where(mask, -jnp.finfo(sim.dtype).max, sim)
            attn = jax.nn.softmax(sim, axis=-1)
            out = jnp.einsum('bhwij,bhwjd->bhwid', attn, bv)
            return out.reshape(b, h, n, d)

        def _layer(x, wqkv, qs, ksc, wo, lg, lb, w1, b1, w2, b2):
            b, n, _ = x.shape
            h = shift_token(x)
            qkv = h @ wqkv
            q, k, v = jnp.split(qkv, 3, axis=-1)
            to_heads = lambda t: t.reshape(b, n, HEADS, DIM_HEAD).transpose(0, 2, 1, 3)
            q, k, v = (to_heads(q), to_heads(k), to_heads(v))
            q = l2norm(q) * qs
            k = l2norm(k) * ksc
            q, k = rotary_xpos(q, k)
            o = local_attention(q, k, v)
            o = o.transpose(0, 2, 1, 3).reshape(b, n, INNER)
            x = x + o @ wo
            h = shift_token(x)
            mu = h.mean(-1, keepdims=True)
            var = h.var(-1, keepdims=True)
            h = (h - mu) / jnp.sqrt(var + 1e-05) * lg + lb
            h = h @ w1 + b1
            a, g = jnp.split(h, 2, axis=-1)
            h = a * jax.nn.gelu(g, approximate=False)
            x = x + h @ w2 + b2
            return x
        for l in range(DEPTH):
            x = _layer(x, wqkv[l], q_scale[l], k_scale[l], wo[l], ln_g[l], ln_b[l], w1[l], b1[l], w2[l], b2[l])
        return x
    x = L0_attn_x
    mod = (_silu(L0_c) @ L0_wmod).reshape(L0_c.shape[0], 6, 1, -1)
    sa, ca, ga, sb, cb, gb = (mod[:, 0], mod[:, 1], mod[:, 2], mod[:, 3], mod[:, 4], mod[:, 5])
    ga = (2 * (ga >= 0) - 1) * jnp.maximum(jnp.abs(ga), 0.25)
    gb = (2 * (gb >= 0) - 1) * jnp.maximum(jnp.abs(gb), 0.25)
    h = _layernorm(x, axis=-1) * (1 + ca) + sa
    x = x + ga * _L0_attn_ref(h, L0_attn_W_DKV, L0_attn_W_UK, L0_attn_W_UV, L0_attn_W_UQ, L0_attn_W_O)
    h = _layernorm(x, axis=-1) * (1 + cb) + sb
    x = x + gb * _L0_ffn_ref(h, L0_ffn_wqkv, L0_ffn_q_scale, L0_ffn_k_scale, L0_ffn_wo, L0_ffn_ln_g, L0_ffn_ln_b, L0_ffn_w1, L0_ffn_b1, L0_ffn_w2, L0_ffn_b2)
    return x

_drawn_inputs = setup_inputs


def setup_inputs(seed=0):
    import zlib

    import numpy as np

    out = dict(_drawn_inputs(seed))
    spreads = {'L0_ffn_q_scale': (1.0, 0.6),
     'L0_ffn_k_scale': (1.0, 0.6),
     'L0_ffn_ln_g': (1.0, 0.6),
     'L0_ffn_ln_b': (0.0, 0.8),
     'L0_ffn_b1': (0.0, 0.8),
     'L0_ffn_b2': (0.0, 0.78)}
    factors = {'L0_attn_W_DKV': 8.0,
     'L0_attn_W_UK': 8.0,
     'L0_attn_W_UV': 8.0,
     'L0_attn_W_UQ': 8.0,
     'L0_attn_W_O': 8.0,
     'L0_ffn_wqkv': 7.653,
     'L0_ffn_wo': 7.653,
     'L0_ffn_w1': 8.0,
     'L0_ffn_w2': 8.0}
    for name, (base, spread) in spreads.items():
        noise = np.random.default_rng([zlib.crc32(name.encode()), seed]).standard_normal(out[name].shape)
        drawn = base * np.exp(spread * noise) if base else spread * noise
        out[name] = jnp.asarray(drawn.astype(out[name].dtype))
    for name, factor in factors.items():
        out[name] = (out[name] * factor).astype(out[name].dtype)
    return out
```

```python
from contextlib import ExitStack

import concourse.bass as bass
import numpy as np
from concourse import mybir

F32 = mybir.dt.float32
BF16 = mybir.dt.bfloat16
ALU = mybir.AluOpType
ACT = mybir.ActivationFunctionType
AX_X = mybir.AxisListType.X

P = 128
T = 512
NT = T // P
B = 16
H1, D1 = 16, 8
SLOTS = 8
H2, D2 = 8, 64
NP2 = H2 // 2
BAND = 192
HID = 341
CH = [(0, 128), (128, 128), (256, 85)]
DEPTH = 2
EPS = 1e-5
EXP_AND_LN = "natural_log_exp_and_others"
MASKED = -1e37
SC1 = float(D1) ** -0.5
QK_SCALE = 8.0
NORM_SCALE = 2.0 ** 20
S2 = 2
OFF = [0, 512, 896, 1152]
MAX_UNITS = ([(0, h, 8) for h in (0, 8)] + [(1, h, 4) for h in range(0, H1, 4)]
             + [(2, h, 2) for h in range(0, H1, 2)] + [(3, h, 2) for h in range(0, H1, 2)])
Q_PART = [0, 1, 2, 0, 1, 2, 0, 1]
K_PART = [1, 2, 0, 2, 0, 1, 0, 1]
Q_HELD, K_HELD = [0, 1, 2], [0, 1, 2, 0, 1]
Q_RUNS, K_RUNS = [(0, 3, 0), (3, 3, 0), (6, 2, 0)], [(0, 3, 1), (3, 3, 2), (6, 2, 0)]
for parts, held, runs in ((Q_PART, Q_HELD, Q_RUNS), (K_PART, K_HELD, K_RUNS)):
    assert len(parts) == SLOTS
    assert parts == [held[at + i] for _, count, at in runs for i in range(count)]


SHIFTS = {("spread", 1): 0, ("wout", 0): 1, ("down", 0): 2, ("wout", 1): 3}


def steps():
    out = [("load",), ("center", 0), ("spread", 0), ("proj",)]
    out += [("max", u) for u in range(len(MAX_UNITS))] + [("rows", 0)]
    for g in range(H1 // 4):
        out += [("score", 4 * g + j) for j in range(4)] + [("ctx", g), ("turn", g)]
    out += [("join",), ("out",), ("center", 1), ("spread", 1)]
    for l in range(DEPTH):
        for t in range(NT + 2):
            out += [("qkv", l, t)] * (t < NT) + [("norm", l, t - 1)] * (1 <= t <= NT) + [("heads", l, t - 2)] * (t >= 2)
        out += [("wmax", l, h) for h in range(H2)] + [("rows", l + 1)]
        for p in range(NP2 + 1):
            out += [("wscore", l, 2 * p + r) for r in range(2) if p < NP2] + [("wctx", l, p - 1)] * (p > 0)
        out += [("wout", l), ("center", 2 + l), ("spread", 2 + l)]
        out += [("hid", l, c) for c in range(3)] + [("down", l)]
    return out + [("final",)]


ORDER = [(s, name) for name in steps() for s in range(S2)]


class Ring:

    def __init__(self, banks, full):
        self.banks, self.full = banks, full
        self.n, self.last, self.used = [0] * len(banks), [[] for _ in banks], {}
        self.turn = 0

    def take(self, pe, key, readers):
        k = self.turn % len(self.banks)
        self.turn += 1
        for sem, count in self.last[k]:
            pe.wait_ge(sem, count)
        self.last[k] = readers
        self.n[k] += 1
        self.used[key] = (k, self.n[k])
        return self.banks[k], self.full[k]

    def wait(self, eng, key):
        k, n = self.used[key]
        eng.wait_ge(self.full[k], n)
        return self.banks[k]


def build(nc, x, wdkv, wuk, wuv, wuq, wo1, wqkv, q_scale, k_scale, wo, ln_g, ln_b, w1, b1, w2, b2,
          cond, wmod, c_f32, c_bits, c_rot, out):
    with ExitStack() as ctx:
        def sb(name, shape, dt=F32):
            return ctx.enter_context(nc.sbuf_tensor(name, shape, dt))

        def sem(name):
            return ctx.enter_context(nc.semaphore(name))

        def sems(name):
            return [sem(f"{name}{s}") for s in range(S2)]

        cf = sb("cf", [P, 3, P])
        ident, centre, mean = cf[:, 0, :], cf[:, 1, :], cf[:, 2, :]
        cb = sb("cb", [P, 3 * P + 3 * BAND], BF16)
        identb, causal, causal_t = (cb[:, i * P:(i + 1) * P] for i in range(3))
        band_first, band, band_t = (cb[:, 3 * P + i * BAND:3 * P + (i + 1) * BAND] for i in range(3))
        pick = sb("pick", [2 * H1, H1, P], BF16)
        ones = sb("ones", [P, D2])
        Wq = sb("Wq", [P, P])
        Wk = sb("Wk", [P, P])
        Wv = sb("Wv", [P, P])
        Wo1 = sb("Wo1", [P, P])
        Wqkv = sb("Wqkv", [P, DEPTH, 3 * T])
        Wo = sb("Wo", [P, DEPTH, NP2, P])
        W1 = sb("W1", [P, DEPTH, 2 * HID])
        W2 = sb("W2", [P, DEPTH, 3, P])
        B1 = sb("B1", [P, DEPTH, 2, 3])
        B2 = sb("B2", [P, DEPTH])
        rot = sb("rot", [P, DEPTH, 2, NT, 2, D2])
        mod = sb("mod", [P, 6, B])
        eps = sb("eps", [P, 2])
        vec = sb("vec", [P, 4 * B + 2 * DEPTH])

        xn = [sb(f"xn{s}", [P, NT, P]) for s in range(S2)]
        xT = [sb(f"xT{s}", [P, T]) for s in range(S2)]
        hT = [sb(f"hT{s}", [P, T]) for s in range(S2)]
        hs = [sb(f"hs{s}", [P, T]) for s in range(S2)]
        y = [sb(f"y{s}", [P, T]) for s in range(S2)]
        Q = [sb(f"Q{s}", [P, NP2 * T]) for s in range(S2)]
        K = [sb(f"K{s}", [P, H2 * T]) for s in range(S2)]
        V = [sb(f"V{s}", [P, NT * T]) for s in range(S2)]
        qb = [sb(f"qb{s}", [P, NP2, T], BF16) for s in range(S2)]
        kb = [sb(f"kb{s}", [P, NP2, T], BF16) for s in range(S2)]
        pr = [sb(f"pr{s}", [P, 4, 1280]) for s in range(S2)]
        scr = [sb(f"scr{s}", [P, 2560]) for s in range(S2)]
        cur = [sb(f"cur{s}", [P, 6]) for s in range(S2)]
        nm = [sb(f"nm{s}", [P, NT, H1]) for s in range(S2)]
        nmb = [sb(f"nmb{s}", [P, NT, 2, H1], BF16) for s in range(S2)]
        mT = [sb(f"mT{s}", [2 * H1, T], BF16) for s in range(S2)]
        nrm = [a[:, 0:3 * 4 * H2].rearrange("p (t j h) -> p t j h", t=3, j=2) for a in scr]
        rec = [sb(f"rec{s}", [P, NT, 4])[:, :, :] for s in range(S2)]

        Q1 = [a[:, :].bitcast(BF16).rearrange("p (h n) -> p h n", n=T) for a in Q]
        K1 = [a[:, :].bitcast(BF16).rearrange("p (h n) -> p h n", n=T) for a in K]
        V1 = [a[:, 0:NT * H1 * 16].rearrange("p (t h c) -> p t h c", t=NT, c=16) for a in V]
        Q2 = [a[:, :].rearrange("p (h n) -> p h n", n=T) for a in Q]
        K2 = [a[:, :].rearrange("p (r h n) -> p r h n", r=2, n=T) for a in K]
        V2 = [a[:, :].rearrange("p (t n) -> p t n", n=T) for a in V]
        parts = [[a[:, i * 256:(i + 1) * 256].bitcast(BF16) for i in range(6)] for a in scr]
        rest = [[a[:, 1536 + i * T:1536 + (i + 1) * T] for i in range(2)] for a in scr]
        cg = [a[:, 0:4 * T].rearrange("p (g n) -> p g n", n=T) for a in scr]
        cn = [a[:, 4 * T:5 * T].rearrange("p (t c) -> p t c", c=P) for a in scr]
        flat = [a[:, :, :].rearrange("p a n -> p (a n)") for a in pr]
        t1 = [[a[:, i * 2 * T:(i + 1) * 2 * T] for i in range(3)] for a in flat]
        t2 = [a[:, 6 * T:8 * T] for a in flat]
        sqk = [a[:, 8 * T:10 * T] for a in flat]
        sq = [a[:, 3 * T:4 * T] for a in scr]
        rs = [a[:, 4 * T:5 * T] for a in scr]
        ctx2 = [a[:, 0:4 * T].rearrange("p (h n) -> p h n", n=T) for a in scr]
        rden = [a[:, 4 * T:5 * T] for a in scr]
        hid = [a[:, 0:3 * T].rearrange("p (c n) -> p c n", n=T) for a in scr]
        gel = [a[:, 3 * T:5 * T].rearrange("p (c n) -> p c n", n=T) for a in scr]

        def k1(s, h):
            return K1[s][:, (h % 2) * (H1 // 2) + h // 2, :]

        psw = ctx.enter_context(nc.psum_tensor("psw", [P, 2, 2 * T], F32))
        psz = ctx.enter_context(nc.psum_tensor("psz", [P, 4, T], F32))

        qd = nc.dram_tensor("qd", [S2, H1, len(Q_HELD), D1, T], BF16, kind="Internal").ap()
        kd = nc.dram_tensor("kd", [S2, H1, len(K_HELD), D1, T], BF16, kind="Internal").ap()

        loaded = sem("loaded")
        setup_dve = sem("setup_dve")
        setup_pe = sem("setup_pe")
        setup_act = sem("setup_act")
        x_in = sems("x_in")
        first = sem("first")
        w_full = [sem(f"w_full{i}") for i in range(2)]
        z_full = [sem(f"z_full{i}") for i in range(4)]
        cur_r = sems("cur_r")
        xt_r = sems("xt_r")
        xc_r = sems("xc_r")
        sq_r = sems("sq_r")
        rs_r = sems("rs_r")
        y_r = sems("y_r")
        ym_r = sems("ym_r")
        hi_r = sems("hi_r")
        res_r = sems("res_r")
        mid_r = sems("mid_r")
        lo_r = sems("lo_r")
        v1_r = sems("v1_r")
        vone_r = sems("vone_r")
        spread_w = [sems("spread_q"), sems("spread_k")]
        spread_r = sems("spread_r")
        nm_r = sems("nm_r")
        nmh_r = sems("nmh_r")
        nml_r = sems("nml_r")
        mt_r = sems("mt_r")
        ex_r = sems("ex_r")
        cg_r = sems("cg_r")
        rec_r = sems("rec_r")
        cn_r = sems("cn_r")
        ct_r = sems("ct_r")
        x1_r = sems("x1_r")
        hsa_r = sems("hsa_r")
        hsp_r = sems("hsp_r")
        sqk_r = sems("sqk_r")
        ss_r = sems("ss_r")
        nrm_r = sems("nrm_r")
        t_r = sems("t_r")
        sum_r = sems("sum_r")
        rot_r = sems("rot_r")
        v2_r = sems("v2_r")
        qt_r = sems("qt_r")
        kt_r = sems("kt_r")
        qb_r = sems("qb_r")
        kb_r = sems("kb_r")
        we_r = sems("we_r")
        rd_r = sems("rd_r")
        c2_r = sems("c2_r")
        hres_r = sems("hres_r")
        ge_r = sems("ge_r")
        hid_r = sems("hid_r")
        fin_r = sems("fin_r")
        on_r = sems("on_r")
        stored = sems("stored")
        last = sem("last")
        once = range(first.num, last.num + 1)

        w = Ring([psw[:, i, :] for i in range(2)], w_full)
        z = Ring([psz[:, i, :] for i in range(4)], z_full)

        x_v = x.rearrange("b (t p) c -> b p t c", p=P)
        out_v = out.rearrange("b (t p) c -> b p t c", p=P)
        ITERS = B // S2
        LOADS = 15 + 13 * DEPTH
        loads = []


        dkv = xn[0][:, 0, 0:32]
        uk = xn[0][0:32, 1, :]
        uv = xn[0][0:32, 2, :]
        dkvT = xn[0][0:32, 3, :]
        rot_raw = pr[0][:, :, :].rearrange("p a n -> p (a n)")[:, 0:NT * 4 * D2].rearrange(
            "p (t j d) -> p t j d", t=NT, j=4)
        scl = scr[0][:, 0:DEPTH * 2 * D2].rearrange("p (l j d) -> p l j d", l=DEPTH, j=2)
        cnat = scr[0][0:B, 512:640]
        cT = scr[0][:, 640:656]
        ce = scr[0][:, 656:672]
        cr = scr[0][:, 672:688]
        csil = scr[0][:, 688:704]
        wm = V[0][:, 0:6 * P]
        gab = vec[:, 0:2 * B].rearrange("p (j b) -> p j b", j=2)
        gsg = vec[:, 2 * B:4 * B].rearrange("p (j b) -> p j b", j=2)
        lgb = vec[:, 4 * B:4 * B + 2 * DEPTH].rearrange("p (l j) -> p l j", j=2)

        with nc.Block() as block:
            @block.tensor
            def _(pe):
                pe.wait_ge(loaded, 16 * LOADS)
                pe.wait_ge(setup_dve, 1)
                pe.transpose(psz[0:32, 0, 0:P], dkv, ident).then_inc(setup_pe, 1)
                pe.transpose(psz[:, 1, 0:B], cnat, ident[0:B, 0:B]).then_inc(setup_pe, 1)
                pe.wait_ge(setup_act, 2)
                pe.matmul(psz[:, 2, 0:P], dkvT, uk, start=True, stop=True).then_inc(setup_pe, 1)
                pe.matmul(psz[:, 3, 0:P], dkvT, uv, start=True, stop=True).then_inc(setup_pe, 1)
                pe.wait_ge(setup_dve, 4)
                for j in range(6):
                    mm = pe.matmul(psw[:, 0, j * B:(j + 1) * B], wm[:, j * P:(j + 1) * P], csil, start=True, stop=True)
                mm.then_inc(setup_pe, 1)
                for l in range(DEPTH):
                    for j in range(2):
                        for c, (c0, cn_) in enumerate(CH):
                            i = (l * 2 + j) * 3 + c
                            o = j * HID + c0
                            mm = pe.matmul(psw[0:cn_, 1, 2 * i:2 * i + 1], W1[:, l, o:o + cn_], lgb[:, l, 1:2],
                                           start=True, stop=True)
                mm.then_inc(setup_pe, 1)

            @block.scalar
            def _(act):
                act.wait_ge(setup_pe, 2)
                act.activation(dkvT, psz[0:32, 0, 0:P], ACT.Copy).then_inc(setup_act, 1)
                act.activation(cT, psz[:, 1, 0:B], ACT.Copy).then_inc(setup_act, 1)
                act.activation(ce, psz[:, 1, 0:B], ACT.Exp, scale=-1.0).then_inc(setup_act, 1)
                act.wait_ge(setup_pe, 4)
                act.activation(Wk[:, :], psz[:, 2, 0:P], ACT.Copy).then_inc(setup_act, 1)
                act.activation(Wv[:, :], psz[:, 3, 0:P], ACT.Copy).then_inc(setup_act, 1)

            @block.vector
            def _(dve):
                for i in range(2):
                    dve.memset(psw[:, i, :], 0.0)
                dve.memset(psz[:, :, :].rearrange("p a n -> p (a n)"), 0.0).then_inc(setup_dve, 1)
                dve.wait_ge(loaded, 16 * LOADS)
                dve.wait_ge(setup_act, 3)
                dve.tensor_scalar(ce, ce, 1.0, None, ALU.add).then_inc(setup_dve, 1)
                dve.wait_ge(setup_dve, 2)
                dve.reciprocal(cr, ce).then_inc(setup_dve, 1)
                dve.wait_ge(setup_dve, 3)
                dve.tensor_tensor(csil, cT, cr, ALU.mult).then_inc(setup_dve, 1)
                for l in range(DEPTH):
                    for j in range(2):
                        sc = scl[:, l, j, :].unsqueeze(1).broadcast_to([P, NT, D2])
                        dve.tensor_tensor(rot[:, l, 0, :, j, :], rot_raw[:, :, 2 * j, :], sc, ALU.mult)
                        for half in range(2):
                            o, q = half * 32, (1 - half) * 32
                            dve.tensor_tensor(rot[:, l, 1, :, j, o:o + 32], rot_raw[:, :, 2 * j + 1, o:o + 32],
                                              scl[:, l, j, q:q + 32].unsqueeze(1).broadcast_to([P, NT, 32]), ALU.mult)
                dve.wait_ge(setup_pe, 6)
                dve.tensor_copy(mod[:, :, :].rearrange("p j b -> p (j b)"), psw[:, 0, 0:6 * B]).then_inc(setup_dve, 1)
                dve.wait_ge(setup_dve, 5)
                gates = mod[:, 2::3, :]
                dve.tensor_scalar(gsg, gates, 0.0, None, ALU.is_ge).then_inc(setup_dve, 1)
                dve.wait_ge(setup_dve, 6)
                dve.tensor_scalar(gsg, gsg, 2.0, -1.0, ALU.mult, ALU.add).then_inc(setup_dve, 1)
                dve.wait_ge(setup_dve, 7)
                dve.tensor_tensor(gab, gates, gsg, ALU.mult).then_inc(setup_dve, 1)
                dve.wait_ge(setup_dve, 8)
                dve.tensor_scalar(gab, gab, 0.25, None, ALU.max).then_inc(setup_dve, 1)
                dve.wait_ge(setup_dve, 9)
                dve.tensor_tensor(gates, gab, gsg, ALU.mult).then_inc(setup_dve, 1)
                dve.tensor_scalar(mod[:, 1::3, :], mod[:, 1::3, :], 1.0, None, ALU.add).then_inc(setup_dve, 1)
                for l in range(DEPTH):
                    for j in range(2):
                        for c, (c0, cn_) in enumerate(CH):
                            i = (l * 2 + j) * 3 + c
                            b = B1[0:cn_, l, j, c:c + 1]
                            dve.tensor_tensor(b, psw[0:cn_, 1, 2 * i:2 * i + 1], b, ALU.add)
                    dve.tensor_scalar(W1[:, l, :], W1[:, l, :], lgb[:, l, 0:1], None, ALU.mult)
                dve.drain().then_inc(setup_dve, 1)

            @block.gpsimd
            def _(pool):
                pool.memset(ones[:, :], 1.0)
                pool.memset(eps[:, 0:1], EPS)
                pool.memset(eps[:, 1:2], float(np.log(NORM_SCALE) / 2))
                for s in range(S2):
                    pool.memset(hs[s][:, :], 0.0)
                    pool.memset(K[s][:, :], 0.0)
                    pool.memset(nm[s][:, :, :].rearrange("p a n -> p (a n)"), 0.0)

            @block.sync
            def _(sp):
                def load(dst, src):
                    loads.append(0)
                    sp.dma_start(dst, src).then_inc(loaded, 16)

                load(cf[:, :, :], c_f32)
                c_bf = c_bits.bitcast(BF16)
                load(cb[:, :], c_bf[:, 0:3 * P + 3 * BAND])
                o = 3 * P + 3 * BAND
                load(pick[:, :, :].rearrange("p h n -> p (h n)"), c_bf[0:2 * H1, o:o + H1 * P])
                load(rot_raw, c_rot)
                load(dkv, wdkv)
                load(uk, wuk)
                load(uv, wuv)
                load(Wq[:, :], wuq)
                load(Wo1[:, :], wo1)
                load(cnat, cond)
                load(wm, wmod)
                load(scl[:, :, 0, :], q_scale.unsqueeze(0).broadcast_to([P, DEPTH, D2]))
                load(scl[:, :, 1, :], k_scale.unsqueeze(0).broadcast_to([P, DEPTH, D2]))
                load(Wqkv[:, :, :], wqkv.rearrange("l c n -> c l n"))
                load(W1[:, :, :], w1.rearrange("l c n -> c l n"))
                for l in range(DEPTH):
                    load(lgb[:, l, 0:1], ln_g[l].unsqueeze(1))
                    load(lgb[:, l, 1:2], ln_b[l].unsqueeze(1))
                    load(B2[:, l:l + 1], b2[l].unsqueeze(1))
                    for c, (c0, cn_) in enumerate(CH):
                        load(W2[0:cn_, l, c, :], w2[l, c0:c0 + cn_, :])
                        for j in range(2):
                            load(B1[0:cn_, l, j, c:c + 1], b1[l, j * HID + c0:j * HID + c0 + cn_].unsqueeze(1))
                    load(Wo[:, l, :, :], wo[l].rearrange("(a p) n -> p a n", p=P))
                assert len(loads) == LOADS, len(loads)
                sp.wait_ge(setup_dve, 12)
                sp.wait_ge(setup_act, 5)
                for s in range(S2):
                    sp.dma_start(xn[s][:, :, :], x_v[s]).then_inc(x_in[s], 16)

        with nc.Fori(0, ITERS) as it:
            with nc.Block() as block:
                @block.tensor
                def _(pe):
                    def transposes(dst, src):
                        for t in range(NT):
                            mm = pe.transpose(dst[:, t * P:(t + 1) * P], src(t), ident)
                        return mm

                    def step(s, kind, *a):
                        if kind == "load":
                            bank, full = z.take(pe, (s, "xT"), [(xt_r[s], 1)])
                            transposes(bank, lambda t: xn[s][:, t, :]).then_inc(full, 1)
                        elif kind == "center":
                            n, = a
                            if n == 0:
                                pe.wait_ge(xt_r[s], 1)
                            elif n == 1:
                                pe.wait_ge(x1_r[s], 1)
                            else:
                                pe.wait_ge(hsa_r[s], 2 * (n - 2) + 2)
                                pe.wait_ge(hsp_r[s], 2 * (n - 2) + 2)
                            bank, full = z.take(pe, (s, "xc", n), [(sq_r[s], n + 1)])
                            pe.matmul(bank, centre, (xT if n < 2 else hs)[s][:, :], start=True, stop=True).then_inc(full, 1)
                        elif kind == "spread":
                            n, = a
                            bank, full = z.take(pe, (s, "var", n), [(rs_r[s], 2 * n + 1)])
                            pe.wait_ge(sq_r[s], n + 1)
                            pe.matmul(bank, mean, sq[s], start=True, stop=True).then_inc(full, 1)
                        elif kind == "proj":
                            pe.wait_ge(ym_r[s], 1)
                            for i, wt in enumerate((Wq, Wk)):
                                bank, full = z.take(pe, (s, "qk", i), [(hi_r[s], i + 1), (res_r[s], i + 1)])
                                pe.matmul(bank, wt[:, :], y[s][:, :], start=True, stop=True).then_inc(full, 1)
                            bank, full = z.take(pe, (s, "v"), [(v1_r[s], 1)])
                            for t in range(NT):
                                mm = pe.matmul(bank[:, t * P:(t + 1) * P], y[s][:, t * P:(t + 1) * P], Wv[:, :],
                                               start=True, stop=True)
                            mm.then_inc(full, 1)
                        elif kind == "max":
                            u, = a
                            qt, h0, n = MAX_UNITS[u]
                            wd = (qt + 1) * P
                            bank, full = w.take(pe, (s, "max", u), [(nm_r[s], u + 1)])
                            if u == 0:
                                pe.wait_ge(spread_r[s], 16 * 2 * (len(Q_RUNS) + len(K_RUNS)))
                            per = max(T // wd, 1) if wd != 384 else 1
                            for i in range(n):
                                h = h0 + i
                                o = (i // per) * T + (i % per) * wd
                                lhs = Q1[s][:, h // 2, qt * P:(qt + 1) * P]
                                if qt:
                                    pe.matmul(bank[:, o:o + wd - P], lhs, k1(s, h)[:, 0:wd - P], start=True, stop=True)
                                last_tile = bank[:, o + wd - P:o + wd]
                                pe.matmul(last_tile, lhs, k1(s, h)[:, wd - P:wd], start=True, stop=False)
                                mm = pe.matmul(last_tile, identb, causal, start=False, stop=True)
                            mm.then_inc(full, 1)
                        elif kind == "rows":
                            n, = a
                            bank, full = z.take(pe, (s, "rows", n), [(mt_r[s], n + 1)])
                            pe.wait_ge(nml_r[s], n + 1)
                            for t in range(NT):
                                mm = pe.transpose(bank[0:2 * H1, t * 64:(t + 1) * 64].bitcast(BF16),
                                                  nmb[s][:, t, :, :].rearrange("p a h -> p (a h)"), identb)
                            mm.then_inc(full, 1)
                        elif kind == "score":
                            h, = a
                            if h == 0:
                                pe.wait_ge(mt_r[s], 1)

                            def scores(dst, hd, kt):
                                q0 = kt * P
                                pe.matmul(dst, k1(s, hd)[:, q0:q0 + P], Q1[s][:, hd // 2, q0:T], start=True, stop=False)
                                pe.matmul(dst[:, 0:P], identb, causal_t, start=False, stop=False)
                                return pe.matmul(dst, pick[:, hd, :], mT[s][:, q0:T], start=False, stop=True)

                            i = 3 * (h // 2) + h % 2
                            bank, full = w.take(pe, (s, "sa", h), [(ex_r[s], i + 1)])
                            scores(bank[:, 0:512], h, 0)
                            scores(bank[:, 512:896], h, 1).then_inc(full, 1)
                            if h % 2:
                                bank, full = w.take(pe, (s, "sb", h), [(ex_r[s], i + 2)])
                                for j in range(2):
                                    scores(bank[:, j * T:j * T + 256], h - 1 + j, 2)
                                    mm = scores(bank[:, j * T + 256:j * T + 384], h - 1 + j, 3)
                                mm.then_inc(full, 1)
                        elif kind == "ctx":
                            g, = a
                            bank, full = z.take(pe, (s, "ctx", g), [(cg_r[s], g + 1)])
                            if g == 0:
                                pe.wait_ge(v1_r[s], 1)
                                pe.wait_ge(vone_r[s], 2)
                            pe.wait_ge(ex_r[s], 6 * (g + 1))
                            for kt in range(NT):
                                for j in range(4):
                                    mm = pe.matmul(bank[32 * j:32 * j + 16, kt * P:T], V1[s][:, kt, 4 * g + j, :],
                                                   pr[s][:, j, OFF[kt]:OFF[kt] + T - kt * P],
                                                   start=(kt == 0), stop=(kt == NT - 1))
                            mm.then_inc(full, 1)
                        elif kind == "turn":
                            g, = a
                            bank, full = z.take(pe, (s, "turn", g), [(cn_r[s], g + 1)])
                            pe.wait_ge(cg_r[s], g + 1)
                            transposes(bank, lambda t: cg[s][:, g, t * P:(t + 1) * P]).then_inc(full, 1)
                        elif kind == "join":
                            bank, full = z.take(pe, (s, "join"), [(ct_r[s], 1)])
                            pe.wait_ge(cn_r[s], 4)
                            transposes(bank, lambda t: cn[s][:, t, :]).then_inc(full, 1)
                        elif kind == "out":
                            bank, full = z.take(pe, (s, "out"), [(x1_r[s], 1)])
                            pe.wait_ge(ct_r[s], 1)
                            pe.matmul(bank, Wo1[:, :], y[s][:, :], start=True, stop=True).then_inc(full, 1)
                        elif kind == "qkv":
                            l, t = a
                            if t == 0:
                                pe.wait_ge(hsa_r[s], 2 * l + 1)
                                pe.wait_ge(hsp_r[s], 2 * l + 1)
                            n = NT * l + t + 1
                            lhs = hs[s][:, t * P:(t + 1) * P]
                            bank, full = w.take(pe, (s, "qkv", l, t), [(t_r[s], 3 * n)])
                            pe.matmul(bank[:, 0:T], lhs, Wqkv[:, l, 0:T], start=True, stop=True)
                            pe.matmul(bank[:, T:2 * T], lhs, Wqkv[:, l, T:2 * T], start=True, stop=True).then_inc(full, 1)
                            bank, full = z.take(pe, (s, "v2", l, t), [(v2_r[s], n)])
                            pe.matmul(bank, lhs, Wqkv[:, l, 2 * T:3 * T], start=True, stop=True).then_inc(full, 1)
                        elif kind == "heads":
                            l, t = a
                            n = NT * l + t + 1
                            pe.wait_ge(rot_r[s], n)
                            for i, (nam, r) in enumerate((("qT", [(qt_r[s], n)]), ("kT", [(kt_r[s], 2 * n)]))):
                                bank, full = z.take(pe, (s, nam, l, t), r)
                                transposes(bank, lambda p: t1[s][t % 3][:, i * T + p * P:i * T + (p + 1) * P]).then_inc(full, 1)
                        elif kind == "wmax":
                            l, h = a
                            bank, full = w.take(pe, (s, "wmax", l, h), [(nm_r[s], len(MAX_UNITS) + H2 * l + h + 1)])
                            if h == 0:
                                pe.wait_ge(qb_r[s], NT * (l + 1))
                                pe.wait_ge(kb_r[s], NT * (l + 1))
                            r = slice(D2 * (h % 2), D2 * (h % 2) + D2)
                            for t in range(NT):
                                o = (t // 2) * T + (t % 2) * BAND
                                k0 = max(t * P - D2, 0)
                                wd = (t + 1) * P - k0
                                if t == 0:
                                    pe.matmul(bank[:, o:o + D2], identb, band_first[:, 0:D2], start=True, stop=True)
                                dst = bank[:, o + BAND - wd:o + BAND]
                                pe.matmul(dst, identb, (band if t else band_first)[:, BAND - wd:BAND], start=True, stop=False)
                                mm = pe.matmul(dst, qb[s][r, h // 2, t * P:(t + 1) * P],
                                               kb[s][r, h // 2, k0:k0 + wd], start=False, stop=True)
                            mm.then_inc(full, 1)
                        elif kind == "wscore":
                            l, h = a
                            if h == 0:
                                pe.wait_ge(mt_r[s], l + 2)
                                pe.wait_ge(qt_r[s], NT * (l + 1))
                                pe.wait_ge(kt_r[s], 2 * NT * (l + 1))
                            bank, full = w.take(pe, (s, "wscore", l, h), [(we_r[s], H2 * l + h + 1)])
                            for j in range(NT):
                                o = (j // 2) * T + (j % 2) * BAND
                                wd = min(BAND, T - j * P)
                                dst = bank[:, o:o + wd]
                                pe.matmul(dst, identb, band_t[:, 0:wd], start=True, stop=False)
                                pe.matmul(dst, pick[:, h, :], mT[s][:, j * P:j * P + wd], start=False, stop=False)
                                mm = pe.matmul(dst, K2[s][:, h % 2, h // 2, j * P:(j + 1) * P],
                                               Q2[s][:, h // 2, j * P:j * P + wd], start=False, stop=True)
                            mm = pe.matmul(bank[:, o + wd:o + BAND], identb, band_first[:, 0:BAND - wd],
                                           start=True, stop=True)
                            mm.then_inc(full, 1)
                        elif kind == "wctx":
                            l, p = a
                            n = NP2 * l + p + 1
                            num, num_f = z.take(pe, (s, "num", l, p), [(c2_r[s], n)])
                            den, den_f = z.take(pe, (s, "den", l, p), [(rd_r[s], 2 * n - 1)])
                            if p == 0:
                                pe.wait_ge(v2_r[s], NT * (l + 1))
                            pe.wait_ge(we_r[s], H2 * l + 2 * p + 2)
                            for dst, f, one in ((den, den_f, True), (num, num_f, False)):
                                for j in range(NT):
                                    wd = min(BAND, T - j * P)
                                    for r in range(2):
                                        h = 2 * p + r
                                        lhs = ones[:, :] if one else V2[s][:, j, h * D2:(h + 1) * D2]
                                        mm = pe.matmul(dst[D2 * r:D2 * r + D2, j * P:j * P + wd], lhs,
                                                       pr[s][:, h % 4, j * BAND:j * BAND + wd],
                                                       start=(j == 0), stop=(j == NT - 1), skip_group_check=True)
                                mm.then_inc(f, 1)
                        elif kind == "wout":
                            l, = a
                            bank, full = z.take(pe, (s, "wout", l), [(hres_r[s], 2 * l + 1)])
                            pe.wait_ge(c2_r[s], NP2 * (l + 1))
                            for p in range(NP2):
                                mm = pe.matmul(bank, Wo[:, l, p, :], ctx2[s][:, p, :], start=(p == 0), stop=(p == NP2 - 1))
                            mm.then_inc(full, 1)
                        elif kind == "hid":
                            l, c = a
                            c0, cn_ = CH[c]
                            n = 3 * l + c + 1
                            bank, full = w.take(pe, (s, "hid", l, c), [(ge_r[s], n), (hid_r[s], n)])
                            if c == 0:
                                pe.wait_ge(y_r[s], l + 3)
                            pe.matmul(bank[0:cn_, 0:T], W1[:, l, HID + c0:HID + c0 + cn_], y[s][:, :], start=True, stop=True)
                            pe.matmul(bank[0:cn_, T:2 * T], W1[:, l, c0:c0 + cn_], y[s][:, :],
                                      start=True, stop=True).then_inc(full, 1)
                        elif kind == "down":
                            l, = a
                            bank, full = z.take(pe, (s, "down", l), [(hres_r[s], 2 * l + 2)])
                            for c, (c0, cn_) in enumerate(CH):
                                pe.wait_ge(hid_r[s], 3 * l + c + 1)
                                mm = pe.matmul(bank, W2[0:cn_, l, c, :], hid[s][0:cn_, c, :], start=(c == 0), stop=(c == 2))
                            mm.then_inc(full, 1)
                        elif kind == "final":
                            bank, full = z.take(pe, (s, "final"), [(on_r[s], 1)])
                            pe.wait_ge(fin_r[s], 1)
                            transposes(bank, lambda t: xT[s][:, t * P:(t + 1) * P]).then_inc(full, 1)

                    for s in range(S2):
                        pe.wait_ge(x_in[s], 16 * (it + 1))
                    for s, name in ORDER:
                        step(s, *name)

                @block.scalar
                def _(act):
                    def step(s, kind, *a):
                        if kind == "load":
                            act.activation(xT[s][:, :], z.wait(act, (s, "xT")), ACT.Copy).then_inc(xt_r[s], 1)
                        elif kind == "center":
                            n, = a
                            bank = z.wait(act, (s, "xc", n))
                            act.activation(y[s][:, :], bank, ACT.Copy).then_inc(xc_r[s], 1)
                            act.activation(sq[s], bank, ACT.Square).then_inc(sq_r[s], 1)
                        elif kind == "spread":
                            n, = a
                            act.activation(rs[s], z.wait(act, (s, "var", n)), ACT.Ln, bias=eps[:, 0:1]).then_inc(rs_r[s], 1)
                            act.wait_ge(rs_r[s], 2 * n + 1)
                            act.activation(rs[s], rs[s], ACT.Exp, scale=-0.5).then_inc(rs_r[s], 1)
                        elif kind == "proj":
                            for i in range(2):
                                act.activation(parts[s][3 * i], z.wait(act, (s, "qk", i)), ACT.Copy).then_inc(hi_r[s], 1)
                            src = z.wait(act, (s, "v")).rearrange("p (t h d) -> p t h d", t=NT, h=H1)
                            for t in range(NT):
                                ins = act.activation(V1[s][:, t, :, 0:D1], src[:, t], ACT.Copy)
                            ins.then_inc(v1_r[s], 1)
                        elif kind == "rows":
                            n, = a
                            bank = z.wait(act, (s, "rows", n))
                            act.activation(mT[s][:, :], bank[0:2 * H1, 0:T // 2].bitcast(BF16), ACT.Copy).then_inc(mt_r[s], 1)
                        elif kind == "score":
                            h, = a
                            if h == 4 * (h // 4) and h:
                                z.wait(act, (s, "ctx", h // 4 - 1))
                            bank = w.wait(act, (s, "sa", h))
                            act.activation(pr[s][:, h % 4, 0:896], bank[:, 0:896], ACT.Exp, scale=SC1).then_inc(ex_r[s], 1)
                            if h % 2:
                                bank = w.wait(act, (s, "sb", h)).rearrange("p (j n) -> p j n", j=2)
                                act.activation(pr[s][:, h % 4 - 1:h % 4 + 1, 896:1280], bank[:, :, 0:384], ACT.Exp,
                                               scale=SC1).then_inc(ex_r[s], 1)
                        elif kind == "ctx":
                            g, = a
                            act.activation(cg[s][:, g, :], z.wait(act, (s, "ctx", g)), ACT.Copy).then_inc(cg_r[s], 1)
                        elif kind == "join":
                            act.activation(y[s][:, :], z.wait(act, (s, "join")), ACT.Copy).then_inc(ct_r[s], 1)
                        elif kind == "qkv":
                            l, t = a
                            n = NT * l + t
                            if l or t:
                                act.wait_ge(ss_r[s], 2 * n)
                            act.activation(sqk[s], w.wait(act, (s, "qkv", l, t)), ACT.Square).then_inc(sqk_r[s], 1)
                            act.activation(V2[s][:, t, :], z.wait(act, (s, "v2", l, t)), ACT.Copy).then_inc(v2_r[s], 1)
                        elif kind == "norm":
                            l, t = a
                            n = NT * l + t
                            one = nrm[s][:, t % 3, 1, :]
                            act.wait_ge(ss_r[s], 2 * n + 2)
                            act.activation(one, nrm[s][:, t % 3, 0, :], ACT.Ln, scale=NORM_SCALE).then_inc(nrm_r[s], 1)
                            act.wait_ge(nrm_r[s], 2 * n + 1)
                            act.activation(one, one, ACT.Exp, scale=-0.5, bias=eps[:, 1:2]).then_inc(nrm_r[s], 1)
                        elif kind == "heads":
                            l, t = a
                            cols = slice(t * P, (t + 1) * P)
                            bank = z.wait(act, (s, "qT", l, t)).rearrange("p (h n) -> p h n", n=P)
                            act.activation(Q2[s][:, :, cols], bank, ACT.Copy).then_inc(qt_r[s], 1)
                            bank = z.wait(act, (s, "kT", l, t)).rearrange("p (h n) -> p h n", n=P)
                            act.activation(K2[s][0:D2, 0, :, cols], bank[0:D2], ACT.Copy).then_inc(kt_r[s], 1)
                            act.activation(K2[s][D2:P, 1, :, cols], bank[D2:P], ACT.Copy).then_inc(kt_r[s], 1)
                        elif kind == "wscore":
                            l, h = a
                            if h >= 4 and h % 2 == 0:
                                z.wait(act, (s, "num", l, h // 2 - 2))
                                z.wait(act, (s, "den", l, h // 2 - 2))
                            bank = w.wait(act, (s, "wscore", l, h)).rearrange("p (j n) -> p j n", j=2)[:, :, 0:2 * BAND]
                            dst = pr[s][:, h % 4, 0:4 * BAND].rearrange("p (j n) -> p j n", j=2)
                            act.activation(dst, bank, ACT.Exp, scale=QK_SCALE).then_inc(we_r[s], 1)
                        elif kind == "wctx":
                            l, p = a
                            n = NP2 * l + p
                            if p:
                                act.wait_ge(c2_r[s], n)
                            act.activation(rden[s], z.wait(act, (s, "den", l, p)), ACT.Ln).then_inc(rd_r[s], 1)
                            act.wait_ge(rd_r[s], 2 * n + 1)
                            act.activation(rden[s], rden[s], ACT.Exp, scale=-1.0).then_inc(rd_r[s], 1)
                        elif kind == "hid":
                            l, c = a
                            c0, cn_ = CH[c]
                            bank = w.wait(act, (s, "hid", l, c))
                            if c == 2:
                                act.wait_ge(hid_r[s], 3 * l + 1)
                            act.activation(gel[s][0:cn_, c % 2, :], bank[0:cn_, 0:T], ACT.Gelu,
                                           bias=B1[0:cn_, l, 1, c:c + 1]).then_inc(ge_r[s], 1)
                            if c == 2 and s == S2 - 1:
                                act.preload_act_table_set(EXP_AND_LN)
                        shift = SHIFTS.get((kind, *a))
                        if shift is not None:
                            if shift == 0:
                                act.wait_ge(ym_r[s], 2)
                            else:
                                act.wait_ge(hres_r[s], shift)
                            act.activation(hs[s][0:D2, :], hT[s][0:D2, :], ACT.Copy).then_inc(hsa_r[s], 1)

                    act.preload_act_table_set(EXP_AND_LN)
                    for s, name in ORDER:
                        step(s, *name)

                @block.vector
                def _(dve):
                    def split_max(s, n):
                        k, hi, lo = nm[s][:, :, :], nmb[s][:, :, 0, :], nmb[s][:, :, 1, :]
                        dve.tensor_copy(hi, k).then_inc(nmh_r[s], 1)
                        dve.wait_ge(nmh_r[s], n + 1)
                        dve.tensor_tensor(lo, k, hi, ALU.subtract).then_inc(nml_r[s], 1)

                    def step(s, kind, *a):
                        if kind == "spread":
                            n, = a
                            if n == 0:
                                dve.wait_ge(cur_r[s], 1)
                            dve.wait_ge(rs_r[s], 2 * n + 2)
                            dve.wait_ge(xc_r[s], n + 1)
                            dve.tensor_tensor(y[s][:, :], y[s][:, :], rs[s], ALU.mult).then_inc(y_r[s], 1)
                            if n < 2:
                                dve.wait_ge(y_r[s], n + 1)
                                dst = (y, hT)[n][s]
                                dve.tensor_scalar(dst[:, :], y[s][:, :], cur[s][:, 3 * n + 1:3 * n + 2],
                                                  cur[s][:, 3 * n:3 * n + 1], ALU.mult, ALU.add).then_inc(ym_r[s], 1)
                        elif kind == "proj":
                            for i in range(2):
                                bank = z.wait(dve, (s, "qk", i))
                                dve.wait_ge(hi_r[s], i + 1)
                                dve.tensor_tensor(rest[s][i], bank, parts[s][3 * i], ALU.subtract).then_inc(res_r[s], 1)
                        elif kind == "max":
                            u, = a
                            qt, h0, n = MAX_UNITS[u]
                            wd = (qt + 1) * P
                            bank = w.wait(dve, (s, "max", u))
                            if qt < 2:
                                src = bank[:, 0:n * wd].rearrange("p (h n) -> p h n", n=wd)
                            else:
                                src = bank.rearrange("p (h n) -> p h n", n=T)[:, :, 0:wd]
                            dve.tensor_reduce(nm[s][:, qt, h0:h0 + n], src, AX_X, ALU.max, negate=True).then_inc(nm_r[s], 1)
                            if u == len(MAX_UNITS) - 1:
                                dve.wait_ge(nm_r[s], u + 1)
                                split_max(s, 0)
                        elif kind == "turn":
                            g, = a
                            bank = z.wait(dve, (s, "turn", g)).rearrange("p (t j c) -> p t j c", t=NT, j=4)
                            if g:
                                dve.wait_ge(cn_r[s], g)
                            dve.reciprocal(rec[s], bank[:, :, :, D1]).then_inc(rec_r[s], 1)
                            dve.wait_ge(rec_r[s], g + 1)
                            dst = cn[s].rearrange("p t (h d) -> p t h d", d=D1)[:, :, 4 * g:4 * g + 4, :]
                            dve.tensor_tensor(dst, bank[:, :, :, 0:D1],
                                              rec[s].unsqueeze(3).broadcast_to([P, NT, 4, D1]),
                                              ALU.mult).then_inc(cn_r[s], 1)
                        elif kind == "out":
                            bank = z.wait(dve, (s, "out"))
                            dve.scalar_tensor_tensor(xT[s][:, :], bank, cur[s][:, 2:3], xT[s][:, :], ALU.mult,
                                                     ALU.add).then_inc(x1_r[s], 1)
                        elif kind == "qkv":
                            l, t = a
                            n = NT * l + t
                            i = t % 3
                            bank = w.wait(dve, (s, "qkv", l, t))
                            dve.wait_ge(sqk_r[s], n + 1)
                            if t >= 3:
                                z.wait(dve, (s, "kT", l, t - 3))
                            qk = bank.rearrange("p (j h d) -> p j h d", j=2, h=H2)
                            cos = rot[:, l, 0, t, :, :].unsqueeze(2).broadcast_to([P, 2, H2, D2])
                            dve.tensor_tensor(t1[s][i].rearrange("p (j h d) -> p j h d", j=2, h=H2), qk, cos,
                                              ALU.mult).then_inc(t_r[s], 1)
                            if n:
                                dve.wait_ge(sum_r[s], n)
                            for half in range(2):
                                o, q = half * 32, (1 - half) * 32
                                sin = rot[:, l, 1, t, :, o:o + 32].unsqueeze(2).broadcast_to([P, 2, H2, 32])
                                dve.tensor_tensor(t2[s].rearrange("p (j h d) -> p j h d", j=2, h=H2)[:, :, :, o:o + 32],
                                                  qk[:, :, :, q:q + 32], sin, ALU.mult).then_inc(t_r[s], 1)
                            dve.tensor_reduce(nrm[s][:, i, 0, :], sqk[s].rearrange("p (h d) -> p h d", d=D2), AX_X,
                                              ALU.add).then_inc(ss_r[s], 1)
                            dve.wait_ge(ss_r[s], 2 * n + 1)
                            dve.tensor_scalar(nrm[s][:, i, 0, :], nrm[s][:, i, 0, :], 1e-24, None, ALU.max).then_inc(ss_r[s], 1)
                        elif kind == "norm":
                            l, t = a
                            n = NT * l + t
                            dve.wait_ge(sum_r[s], n + 1)
                            dve.wait_ge(nrm_r[s], 2 * n + 2)
                            v = t1[s][t % 3].rearrange("p (h d) -> p h d", d=D2)
                            dve.tensor_tensor(v, v, nrm[s][:, t % 3, 1, :].unsqueeze(2).broadcast_to([P, 2 * H2, D2]),
                                              ALU.mult).then_inc(rot_r[s], 1)
                        elif kind == "wmax":
                            l, h = a
                            if h == 0:
                                dve.wait_ge(nml_r[s], l + 1)
                            bank = w.wait(dve, (s, "wmax", l, h)).rearrange("p (j n) -> p j n", j=2)
                            src = bank[:, :, 0:2 * BAND].rearrange("p j (i n) -> p j i n", n=BAND)
                            dst = nm[s][:, :, h:h + 1].rearrange("p (j i) h -> p j (i h)", i=2)
                            dve.tensor_reduce(dst, src, AX_X, ALU.max, negate=True).then_inc(nm_r[s], 1)
                            if h == H2 - 1:
                                dve.wait_ge(nm_r[s], len(MAX_UNITS) + H2 * (l + 1))
                                split_max(s, l + 1)
                        elif kind == "wctx":
                            l, p = a
                            n = NP2 * l + p
                            dve.wait_ge(rd_r[s], 2 * n + 2)
                            dve.tensor_tensor(ctx2[s][:, p, :], z.wait(dve, (s, "num", l, p)), rden[s],
                                              ALU.mult).then_inc(c2_r[s], 1)
                        elif kind == "wout":
                            l, = a
                            dve.tensor_tensor(hT[s][:, :], z.wait(dve, (s, "wout", l)), hT[s][:, :],
                                              ALU.add).then_inc(hres_r[s], 1)
                        elif kind == "hid":
                            l, c = a
                            c0, cn_ = CH[c]
                            dve.wait_ge(ge_r[s], 3 * l + c + 1)
                            bank = w.wait(dve, (s, "hid", l, c))
                            dve.scalar_tensor_tensor(hid[s][0:cn_, c, :], bank[0:cn_, T:2 * T], B1[0:cn_, l, 0, c:c + 1],
                                                     gel[s][0:cn_, c % 2, :], ALU.add, ALU.mult).then_inc(hid_r[s], 1)
                        elif kind == "down":
                            l, = a
                            dve.scalar_tensor_tensor(hT[s][:, :], z.wait(dve, (s, "down", l)), B2[:, l:l + 1], hT[s][:, :],
                                                     ALU.add, ALU.add).then_inc(hres_r[s], 1)
                            if l == DEPTH - 1:
                                dve.wait_ge(hres_r[s], 2 * DEPTH)
                                dve.scalar_tensor_tensor(xT[s][:, :], hT[s][:, :], cur[s][:, 5:6], xT[s][:, :], ALU.mult,
                                                         ALU.add).then_inc(fin_r[s], 1)
                        elif kind == "final":
                            dve.tensor_copy(y[s][:, :], z.wait(dve, (s, "final"))).then_inc(on_r[s], 1)
                        shift = SHIFTS.get((kind, *a))
                        if shift is not None:
                            if shift == 0:
                                dve.wait_ge(ym_r[s], 2)
                            else:
                                dve.wait_ge(hres_r[s], shift)
                            dve.tensor_copy(hs[s][D2:P, 1:T], hT[s][D2:P, 0:T - 1]).then_inc(hsp_r[s], 1)

                    for s in range(S2):
                        dve.tensor_copy(cur[s][:, :], mod[:, :, bass.ds(it * S2 + s, 1)].rearrange("p j b -> p (j b)"))\
                            .then_inc(cur_r[s], 1)
                    for s, name in ORDER:
                        step(s, *name)

                @block.gpsimd
                def _(pool):
                    def step(s, kind, *a):
                        if kind == "load":
                            pool.memset(V1[s][:, :, :, D1:16], 0.0).then_inc(vone_r[s], 1)
                            pool.wait_ge(vone_r[s], 1)
                            pool.memset(V1[s][:, :, :, D1:D1 + 1], 1.0).then_inc(vone_r[s], 1)
                        elif kind == "proj":
                            for i in range(2):
                                pool.wait_ge(res_r[s], i + 1)
                                pool.tensor_scalar(parts[s][3 * i + 1], rest[s][i], 1.0, 0.0, ALU.mult,
                                                   ALU.add).then_inc(mid_r[s], 1)
                                pool.wait_ge(mid_r[s], i + 1)
                                pool.tensor_tensor(parts[s][3 * i + 2], rest[s][i], parts[s][3 * i + 1],
                                                   ALU.subtract).then_inc(lo_r[s], 1)
                        elif kind == "qkv":
                            l, t = a
                            pool.wait_ge(t_r[s], 3 * (NT * l + t + 1))
                            pool.tensor_tensor(t1[s][t % 3], t1[s][t % 3], t2[s], ALU.add).then_inc(sum_r[s], 1)
                        elif kind == "heads":
                            l, t = a
                            cols = slice(t * P, (t + 1) * P)
                            n = NT * l + t + 1
                            pool.wait_ge(qt_r[s], n)
                            pool.tensor_scalar(qb[s][:, :, cols], Q2[s][:, :, cols], 1.0, 0.0, ALU.mult,
                                               ALU.add).then_inc(qb_r[s], 1)
                            pool.wait_ge(kt_r[s], 2 * n)
                            pool.tensor_tensor(kb[s][:, :, cols], K2[s][:, 0, :, cols], K2[s][:, 1, :, cols],
                                               ALU.add).then_inc(kb_r[s], 1)

                    for s, name in ORDER:
                        step(s, *name)

                @block.sync
                def _(sp):
                    def step(s, kind, *a):
                        if kind == "proj":
                            for i, (dram, held) in enumerate(((qd, Q_HELD), (kd, K_HELD))):
                                sp.wait_ge(lo_r[s], i + 1)
                                for slot, part in enumerate(held):
                                    sp.dma_start(dram[s, :, slot, :, :], parts[s][3 * i + part]).then_inc(spread_w[i][s], 16)
                            for i, (dram, held, runs) in enumerate(((qd, Q_HELD, Q_RUNS), (kd, K_HELD, K_RUNS))):
                                sp.wait_ge(spread_w[i][s], 16 * len(held))
                                for r in range(2):
                                    for slot, count, at in runs:
                                        rows = slice(64 * r + D1 * slot, 64 * r + D1 * (slot + count))
                                        dst = Q1[s][rows, :, :] if i == 0 else K1[s][rows, r * (H1 // 2):(r + 1) * (H1 // 2), :]
                                        src = dram[s, :, at:at + count].rearrange("(q r) a d n -> (a d) q r n", r=2)
                                        sp.dma_start(dst, src[:, :, r, :]).then_inc(spread_r[s], 16)
                        elif kind == "load":
                            z.wait(sp, (s, "xT"))
                            sp.dma_start(xn[s][:, :, :], x_v[bass.ds((it * S2 + S2 + s) % B, 1)][0]).then_inc(x_in[s], 16)
                        elif kind == "final":
                            sp.wait_ge(on_r[s], 1)
                            sp.dma_start(out_v[bass.ds(it * S2 + s, 1)][0],
                                         y[s][:, :].rearrange("p (t c) -> p t c", c=P)).then_inc(stored[s], 16)

                    for s, name in ORDER:
                        step(s, *name)
                    for s in range(S2):
                        sp.wait_ge(stored[s], 16)
            nc.all_engine_barrier(sems_to_clear=once)

        with nc.Block() as block:
            @block.sync
            def _(sp):
                for s in range(S2):
                    sp.wait_ge(x_in[s], 16 * (ITERS + 1))


def constants():
    eye = np.eye(P, dtype=np.float32)
    c_f32 = np.stack([eye, eye - 1.0 / P, np.full((P, P), 1.0 / P)], 1).astype(np.float32)
    r = np.arange(P)
    causal = np.where(r[None, :] > r[:, None], MASKED, 0.0)
    j = np.arange(BAND)[None, :] - D2
    ok = (r[:, None] >= j) & (r[:, None] <= j + D2)
    band = np.where(ok, 0.0, MASKED)
    first = np.where(ok & (j >= 0), 0.0, MASKED)
    q = np.arange(BAND)[None, :]
    band_t = np.where((q >= r[:, None]) & (q <= r[:, None] + D2), 0.0, MASKED)

    def selectors(h):
        e = np.zeros((P, h, P))
        for i in range(h):
            e[i, i] = e[h + i, i] = 1.0
        return e.reshape(P, h * P)

    c_bf = np.concatenate([eye, causal, causal.T, first, band, band_t, selectors(H1)], 1).astype(np.float32)
    c_bf = (np.ascontiguousarray(c_bf).view(np.uint32) >> 16).astype(np.uint16)
    half = np.arange(0, D2, 2, dtype=np.float32)
    inv = (1.0 / np.float32(10000.0) ** (half / np.float32(D2))).astype(np.float32)
    t = np.arange(T, dtype=np.float32)
    fr = t[:, None] * inv[None, :]
    fr = np.concatenate([fr, fr], 1).astype(np.float64)
    base = ((half + 0.4 * D2) / (1.4 * D2)).astype(np.float64)
    scale = base[None, :] ** ((t.astype(np.float64) - T // 2) / 32.0)[:, None]
    scale = np.concatenate([scale, scale], 1)
    sign = np.where(np.arange(D2) < 32, -1.0, 1.0)
    rot = np.stack([np.cos(fr) * scale, sign * np.sin(fr) * scale, np.cos(fr) / scale, sign * np.sin(fr) / scale], 1)
    c_rot = rot.reshape(NT, P, 4, D2).transpose(1, 0, 2, 3).astype(np.float32)
    return c_f32, c_bf, np.ascontiguousarray(c_rot)


_INS = ["L0_attn_x", "L0_attn_W_DKV", "L0_attn_W_UK", "L0_attn_W_UV", "L0_attn_W_UQ", "L0_attn_W_O", "L0_ffn_wqkv",
        "L0_ffn_q_scale", "L0_ffn_k_scale", "L0_ffn_wo", "L0_ffn_ln_g", "L0_ffn_ln_b", "L0_ffn_w1", "L0_ffn_b1",
        "L0_ffn_w2", "L0_ffn_b2", "L0_c", "L0_wmod"]


def kernel(**inputs):
    import concourse.bacc as bacc
    from concourse.bass_utils import run_bass_kernel_spmd

    nc = bacc.Bacc("TRN2", target_bir_lowering=False, num_devices=1)
    arrays, args = {}, []
    given = [(n, np.ascontiguousarray(inputs[n])) for n in _INS]
    given += list(zip(("c_f32", "c_bf", "c_rot"), constants()))
    for name, a in given:
        arrays[f"in_{name}"] = a
        args.append(nc.dram_tensor(f"in_{name}", a.shape, mybir.dt.from_np(a.dtype), kind="ExternalInput").ap())
    out = nc.dram_tensor("out", (B, T, P), F32, kind="ExternalOutput").ap()
    build(nc, *args, out)
    r = run_bass_kernel_spmd(nc, [arrays], core_ids=[0])
    return r.results[0]["out"]
```
